# Optimizing a Trainium2 kernel written in Bass

```python
import numpy as np
import jax
import jax.numpy as jnp

def _softmax(x, axis=-1):
    return jax.nn.softmax(x, axis=axis)

def _gelu(x):
    return jax.nn.gelu(x, approximate=True)

def _silu(x):
    return jax.nn.silu(x)

def _sigmoid(x):
    return jax.nn.sigmoid(x)

def _layernorm(x, axis=-1, eps=1e-05):
    m = jnp.mean(x, axis=axis, keepdims=True)
    v = jnp.var(x, axis=axis, keepdims=True)
    return (x - m) / jnp.sqrt(v + eps)

def _scatter_add(tgt, idx, src, axis=0):
    return tgt.at[idx].add(src)

def _segment_sum(src, seg, n):
    return jax.ops.segment_sum(src, seg, n)
kernel_name = 'mk_adj_resnorm_d1_adj_r2_edb0d5'

def setup_inputs(seed: int=0):
    np.random.seed(seed)
    _w = jnp.asarray

    def _rec_inputs():
        import jax
        import jax.numpy as jnp
        _gk = jax.random.key(seed)
        x = -0.0005207 + 1.001 * jax.random.normal(jax.random.fold_in(_gk, 1), (16, 512, 128), jnp.float32)
        _w = (1.0 + jnp.arange(512, dtype=jnp.float32)) ** (-0.5)
        _w = _w / _w.mean()
        _pij = jnp.clip(0.00390625 * _w[:, None] * _w[None, :], 0.0, 1.0)
        _a = jax.random.uniform(jax.random.fold_in(_gk, 2), (16, 512, 512)) < _pij
        _a = jnp.logical_or(_a, jnp.swapaxes(_a, -1, -2))
        _a = jnp.logical_or(_a, jnp.eye(512, dtype=bool))
        _af = _a.astype(jnp.float32)
        _af = _af * jax.random.uniform(jax.random.fold_in(_gk, 3), (16, 512, 512), jnp.float32, 0.05, 1)
        adj = _af
        return (x, adj)
    x, adj = _rec_inputs()

    def _L0_gnn_setup():
        import jax, jax.numpy as jnp
        import numpy as np
        B, N, F = (8, 512, 128)
        OUT, REL = (128, 16)
        NADJ = 7
        key = jax.random.key(seed)
        k0, k1, k2, k3, k4 = jax.random.split(key, 5)
        features = jax.random.normal(k0, (B, N, F), dtype=jnp.float32)
        A1 = jax.random.uniform(k1, (B, N, N), dtype=jnp.float32)
        A2 = jax.random.uniform(k2, (B, N, N), dtype=jnp.float32)
        W = jax.random.normal(k3, (NADJ, F + REL, OUT), dtype=jnp.float32) * 0.05
        W_edges = jnp.ones((NADJ, REL), dtype=jnp.float32)
        b = jax.random.uniform(k4, (N, OUT), dtype=jnp.float32, minval=-0.05, maxval=0.05)
        return {'features': features, 'A1': A1, 'A2': A2, 'W': W, 'W_edges': W_edges, 'b': b}
    _L0_gnn_all = _L0_gnn_setup()
    _L0_gnn_in = {k: v for k, v in _L0_gnn_all.items() if k in ('W', 'W_edges', 'b')}
    del _L0_gnn_all
    return {'x': x, 'adj': adj, 'L0_gnn_W': _L0_gnn_in['W'], 'L0_gnn_W_edges': _L0_gnn_in['W_edges'], 'L0_gnn_b': _L0_gnn_in['b']}

def reference(x, adj, L0_gnn_W, L0_gnn_W_edges, L0_gnn_b):
    import jax
    import jax.numpy as jnp

    def _L0_gnn_ref(features, A1, A2, W, W_edges, b):
        import jax, jax.numpy as jnp
        import numpy as np
        B, N, F = (8, 512, 128)
        OUT, REL = (128, 16)
        NADJ = 7
        eye = jnp.zeros_like(A1) + jnp.eye(N, dtype=A1.dtype)
        shifted = jnp.roll(eye, 1, axis=0)
        A_fwd = [A1, A2, shifted]
        A_list = A_fwd + [jnp.swapaxes(a, 1, 2) for a in A_fwd]
        A_list.append(eye)
        A = jnp.stack(A_list, axis=0)
        HW = jnp.einsum('bnf,rfo->rbno', features, W[:, :F]) + jnp.einsum('rd,rdo->ro', W_edges, W[:, F:])[:, None, None, :]
        AHW = jnp.einsum('rbnm,rbmo->rbno', A, HW)
        out = jnp.max(AHW, axis=0) + b
        return out
    x = _layernorm(x + _L0_gnn_ref(x, adj, adj, L0_gnn_W, L0_gnn_W_edges, L0_gnn_b), axis=-1)
    return x

_drawn_inputs = setup_inputs


def setup_inputs(seed=0):
    import zlib

    import numpy as np

    out = dict(_drawn_inputs(seed))
    spreads = {'L0_gnn_W_edges': (1.0, 0.2)}
    factors = {}
    for name, (base, spread) in spreads.items():
        noise = np.random.default_rng([zlib.crc32(name.encode()), seed]).standard_normal(out[name].shape)
        drawn = base * np.exp(spread * noise) if base else spread * noise
        out[name] = jnp.asarray(drawn.astype(out[name].dtype))
    for name, factor in factors.items():
        out[name] = (out[name] * factor).astype(out[name].dtype)
    return out
```

```python
from contextlib import ExitStack

import concourse.bass as bass
from concourse import mybir


F32 = mybir.dt.float32
F32R = mybir.dt.float32r
ACT = mybir.ActivationFunctionType
ALU = mybir.AluOpType

P = 128
ROWS = 24
EPS = 1e-5
X_RELS, Z_RELS, Y_RELS = (2, 5, 6), (3, 4), (0, 1)
RELS = X_RELS + Z_RELS + Y_RELS
OUTER = Y_RELS + Z_RELS


def graph_layer(nc, x, adj, W, W_edges, b, ident_d, chunk_d, lo_rows_d, side_d, out):
    GRAPHS, NODES, FEAT = x.shape
    N_REL, K_ALL, OUT = W.shape
    EDGE = K_ALL - FEAT
    C = NODES // P
    NR = len(RELS)
    assert FEAT == P and OUT == P and NODES == 512 and GRAPHS % 2 == 0

    x_d = x.rearrange("g (j p) f -> g p j f", p=P)
    adj_d = adj.rearrange("g (j p) m -> g p j m", p=P)
    out_d = out.rearrange("g (j p) f -> g p j f", p=P)

    ctx = ExitStack()
    with ctx:
        def sb(name, shape, dt=F32):
            return ctx.enter_context(nc.sbuf_tensor(name, shape, dt))

        def bank(name):
            return ctx.enter_context(nc.psum_tensor(name, [P, 512], F32))

        def sem(name):
            return ctx.enter_context(nc.semaphore(name))

        ident = sb("ident", [P, P])
        chunk_mask = sb("chunk_mask", [P, C])
        lo_rows = sb("lo_rows", [P, 1])
        side_mask = sb("side_mask", [EDGE, 2, P])
        w = sb("w", [P, N_REL, OUT])
        w_hi = sb("w_hi", [P, N_REL, OUT], F32R)
        w_lo = sb("w_lo", [P, N_REL, OUT], F32R)
        w_edge = sb("w_edge", [EDGE, N_REL, OUT])
        edges = sb("edges", [EDGE, N_REL])
        edge_lhs = sb("edge_lhs", [EDGE, len(OUTER), P])
        c_hi = sb("c_hi", [P, len(OUTER), OUT], F32R)
        c_rows = sb("c_rows", [P, len(OUTER), OUT], F32R)
        c_col = sb("c_col", [P, len(X_RELS)])
        bias = sb("bias", [P, C, OUT])
        eps = sb("eps", [P, C])
        neg_half = sb("neg_half", [P, C])
        zeros = sb("zeros", [P, 2 * C])

        a = [sb(f"a{n}", [P, C, NODES]) for n in range(2)]
        a_hi = [sb(f"a_hi{n}", [P, C, NODES], F32R) for n in range(2)]
        a_lo = [sb(f"a_lo{n}", [P, C, NODES], F32R) for n in range(2)]
        at_hi = [sb(f"at_hi{n}", [P, C, NODES], F32R) for n in range(2)]
        at_lo = [sb(f"at_lo{n}", [P, C, NODES], F32R) for n in range(2)]
        xs = [sb(f"xs{n}", [P, C, FEAT]) for n in range(2)]
        x_hi = [sb(f"x_hi{n}", [P, C, FEAT], F32R) for n in range(2)]
        x_lo = [sb(f"x_lo{n}", [P, C, FEAT], F32R) for n in range(2)]
        xt_hi = [sb(f"xt_hi{n}", [P, NODES], F32R) for n in range(2)]
        xt_lo = [sb(f"xt_lo{n}", [P, NODES], F32R) for n in range(2)]
        xb = [sb(f"xb{n}", [P, C, FEAT]) for n in range(2)]
        sums = [sb(f"sums{n}", [P, 2 * C]) for n in range(2)]
        sum_parts = [sb(f"sum_parts{n}", [P, P]) for n in range(2)]
        o = [sb(f"o{n}", [P, C, OUT]) for n in range(2)]
        sums_hi = sb("sums_hi", [P, 2 * C], F32R)
        sum_rows = sb("sum_rows", [P, NODES], F32R)
        zt_hi = sb("zt_hi", [P, NODES], F32R)
        zt_lo = sb("zt_lo", [P, NODES], F32R)
        yt_hi = sb("yt_hi", [P, NODES], F32R)
        yt_lo = sb("yt_lo", [P, NODES], F32R)
        best = sb("best", [P, NODES])
        t = sb("t", [P, C, OUT])
        stats = sb("stats", [P, C, 6])
        mean_var = sb("mean_var", [P, C, 2])
        var_eps = sb("var_eps", [P, C])
        rstd = sb("rstd", [P, C])
        neg_mean = sb("neg_mean", [P, C])
        shift = sb("shift", [P, C])

        at_ps = [bank("at_ps0"), bank("at_ps1")]
        z_ps, y_ps = bank("z_ps"), bank("y_ps")
        rel_ps = [bank(f"rel_ps{n}") for n in range(3)]
        misc_ps = bank("misc_ps")

        ident_in = sem("ident_in")
        w_in = sem("w_in")
        consts_in = sem("consts_in")
        x_in = [sem("x_in0"), sem("x_in1")]
        a_in = [sem("a_in0"), sem("a_in1")]
        stored = [sem("stored0"), sem("stored1")]
        w_hi_done = sem("w_hi_done")
        w_lo_done = sem("w_lo_done")
        pads_zero = sem("pads_zero")
        edge_lhs_done = sem("edge_lhs_done")
        c_mm = sem("c_mm")
        c_hi_done = sem("c_hi_done")
        c_done = sem("c_done")
        a_hi_done = sem("a_hi_done")
        a_lo_done = sem("a_lo_done")
        at_tr = sem("at_tr")
        at_hi_done = sem("at_hi_done")
        at_lo_done = sem("at_lo_done")
        x_hi_done = sem("x_hi_done")
        x_lo_done = sem("x_lo_done")
        xb_done = sem("xb_done")
        xt_tr = sem("xt_tr")
        xt_hi_done = sem("xt_hi_done")
        xt_lo_done = sem("xt_lo_done")
        sums_hi_done = sem("sums_hi_done")
        parts_done = sem("parts_done")
        sums_tr = sem("sums_tr")
        sum_rows_done = sem("sum_rows_done")
        z_mm = sem("z_mm")
        zt_hi_done = sem("zt_hi_done")
        zt_lo_done = sem("zt_lo_done")
        y_mm = sem("y_mm")
        yt_hi_done = sem("yt_hi_done")
        yt_lo_done = sem("yt_lo_done")
        rel_mm = sem("rel_mm")
        first_done = sem("first_done")
        max_done = sem("max_done")
        back_tr = sem("back_tr")
        t_done = sem("t_done")
        stats_done = sem("stats_done")
        mean_done = sem("mean_done")
        var_done = sem("var_done")
        rstd_done = sem("rstd_done")
        o_done = sem("o_done")

        block = ctx.enter_context(nc.Block())

        def after(eng, s, value):
            if not isinstance(value, int) or value > 0:
                eng.wait_ge(s, value)

        def graphs(eng, step):
            step(0, 0, True, False)
            with eng.Fori(0, GRAPHS // 2 - 1) as h:
                step(h, 1, True, True)
                step(h + 1, 0, True, True)
            step(GRAPHS // 2 - 1, 1, False, True)

        def following(half, odd):
            return (half + 1, 0) if odd else (half, 1)

        @block.sync
        def _(sp):
            def load(half, odd, graph):
                after(sp, x_lo_done, graph - 1)
                after(sp, xt_tr, graph - 1)
                after(sp, xb_done, graph - 1)
                sp.dma_start(xs[odd][:], x_d[graph]).then_inc(x_in[odd], 16)
                after(sp, a_lo_done, C * (graph - 1))
                after(sp, at_tr, C * (graph - 1))
                sp.dma_start(a[odd][:], adj_d[graph]).then_inc(a_in[odd], 16)

            def store(half, odd, graph):
                after(sp, o_done, C * (graph + 1))
                sp.dma_start(out_d[graph], o[odd][:]).then_inc(stored[odd], 16)

            sp.dma_start(ident[:], ident_d).then_inc(ident_in, 16)
            load(0, 0, 0)
            sp.dma_start(w[:], W[:, 0:FEAT, :].rearrange("r f o -> f r o")).then_inc(w_in, 16)
            sp.dma_start(chunk_mask[:], chunk_d).then_inc(consts_in, 16)
            sp.dma_start(lo_rows[:], lo_rows_d).then_inc(consts_in, 16)
            sp.dma_start(side_mask[:], side_d).then_inc(consts_in, 16)
            sp.dma_start(w_edge[:], W[:, FEAT:K_ALL, :].rearrange("r d o -> d r o")).then_inc(consts_in, 16)
            with nc.allow_non_contiguous_dma(reason="112 numbers"):
                sp.dma_start(edges[:], W_edges.rearrange("r d -> d r")).then_inc(consts_in, 16)
            sp.dma_start(bias[:], b.rearrange("(j p) o -> p j o", p=P)).then_inc(consts_in, 16)
            load(0, 1, 1)
            load(1, 0, 2)
            with sp.Fori(0, GRAPHS // 2 - 2) as h:
                load(h + 1, 1, 2 * h + 3)
                store(h, 0, 2 * h)
                load(h + 2, 0, 2 * h + 4)
                store(h, 1, 2 * h + 1)
            last = GRAPHS // 2 - 1
            load(last, 1, 2 * last + 1)
            for graph in range(2 * last - 2, GRAPHS):
                store(graph // 2, graph % 2, graph)
            for s in stored:
                sp.wait_ge(s, 16 * (GRAPHS // 2))

        @block.scalar
        def _(act):
            def split_a(half, odd, j):
                g = 2 * half + odd
                if j == 0:
                    act.wait_ge(a_in[odd], 16 * (half + 1))
                    after(act, z_mm, g - 1)
                    after(act, parts_done, 2 * (g - 1))
                act.activation(a_hi[odd][:, j, :], a[odd][:, j, :], ACT.Copy,
                               accum_out=sums[odd][:, j:j + 1]).then_inc(a_hi_done, 1)

            def split_at(half, odd, k):
                g = 2 * half + odd
                act.wait_ge(at_tr, C * g + k + 1)
                act.activation(at_hi[odd][:, k, :], at_ps[k % 2][:], ACT.Copy,
                               accum_out=sums[odd][:, C + k:C + k + 1]).then_inc(at_hi_done, 1)

            def split_xt(half, odd):
                act.wait_ge(xt_tr, 2 * half + odd + 1)
                act.activation(xt_hi[odd][:], misc_ps[:], ACT.Copy).then_inc(xt_hi_done, 1)

            def round_x(half, odd):
                act.wait_ge(x_in[odd], 16 * (half + 1))
                after(act, y_mm, 2 * half + odd - 1)
                act.activation(x_hi[odd][:], xs[odd][:], ACT.Copy).then_inc(x_hi_done, 1)

            def normalize(half, odd):
                g = 2 * half + odd
                act.wait_ge(rstd_done, 2 * (g + 1))
                after(act, stored[odd], 16 * half)
                for j in range(C):
                    act.activation(o[odd][:, j, :], t[:, j, :], ACT.Identity, bias=shift[:, j:j + 1],
                                   scale=rstd[:, j:j + 1]).then_inc(o_done, 1)

            round_x(0, 0)
            split_xt(0, 0)
            for j in range(C):
                split_a(0, 0, j)
                split_at(0, 0, j)
            act.wait_ge(w_in, 16)
            act.activation(w_hi[:], w[:], ACT.Copy).then_inc(w_hi_done, 1)

            def step(half, odd, early, late):
                g = 2 * half + odd
                nxt = following(half, odd)
                prev = (half, 0) if odd else (half - 1, 1)
                if early:
                    split_a(*nxt, 0)
                    split_at(*nxt, 0)
                    round_x(*nxt)
                    split_a(*nxt, 1)
                    split_at(*nxt, 1)
                    split_a(*nxt, 2)
                act.wait_ge(z_mm, g + 1)
                act.activation(zt_hi[:], z_ps[:], ACT.Copy).then_inc(zt_hi_done, 1)
                if early:
                    split_a(*nxt, 3)
                    split_at(*nxt, 2)
                    split_at(*nxt, 3)
                act.wait_ge(y_mm, g + 1)
                act.activation(yt_hi[:], y_ps[:], ACT.Copy).then_inc(yt_hi_done, 1)
                act.wait_ge(rel_mm, NR * g + 1)
                if not late:
                    act.wait_ge(c_done, 2)
                act.activation(best[:], rel_ps[0][:], ACT.Identity, bias=c_col[:, 0:1]).then_inc(first_done, 1)
                if early:
                    split_xt(*nxt)
                if late:
                    normalize(*prev)

            graphs(act, step)
            normalize(GRAPHS // 2 - 1, 1)

        @block.vector
        def _(dve):
            def split_at(half, odd, k):
                g = 2 * half + odd
                dve.wait_ge(at_hi_done, C * g + k + 1)
                dve.tensor_tensor(at_lo[odd][:, k, :], at_ps[k % 2][:], at_hi[odd][:, k, :].bitcast(F32),
                                  ALU.subtract).then_inc(at_lo_done, 1)

            def split_xt(half, odd):
                dve.wait_ge(xt_hi_done, 2 * half + odd + 1)
                dve.tensor_tensor(xt_lo[odd][:], misc_ps[:], xt_hi[odd][:].bitcast(F32),
                                  ALU.subtract).then_inc(xt_lo_done, 1)

            for n in range(2):
                dve.memset(sum_parts[n][:], 0.0).then_inc(pads_zero, 1)
            dve.memset(eps[:], EPS).then_inc(pads_zero, 1)
            dve.memset(neg_half[:], -0.5).then_inc(pads_zero, 1)
            dve.memset(zeros[:], 0.0).then_inc(pads_zero, 1)
            split_xt(0, 0)
            for k in range(C):
                split_at(0, 0, k)
            dve.wait_ge(consts_in, 6 * 16)
            for n, r in enumerate(OUTER):
                dve.tensor_scalar(edge_lhs[:, n, :], side_mask[:, 0 if r in Y_RELS else 1, :], edges[:, r:r + 1],
                                  None, ALU.mult).then_inc(edge_lhs_done, 1)
            dve.wait_ge(w_hi_done, 1)
            dve.tensor_tensor(w_lo[:], w[:], w_hi[:].bitcast(F32), ALU.subtract).then_inc(w_lo_done, 1)
            dve.wait_ge(c_mm, 1)
            dve.tensor_copy(c_hi[:], rel_ps[0][:]).then_inc(c_hi_done, 1)
            dve.tensor_copy(c_col[:], rel_ps[1][:, 0:len(X_RELS)]).then_inc(c_done, 1)
            dve.wait_ge(c_hi_done, 1)
            dve.scalar_tensor_tensor(out=c_rows[:], in0=c_hi[:].bitcast(F32), scalar=lo_rows[:],
                                     in1=rel_ps[0][:].rearrange("p (r o) -> p r o", o=OUT),
                                     op0=ALU.mult, op1=ALU.add).then_inc(c_done, 1)

            def take_max(g, q):
                dve.wait_ge(rel_mm, NR * g + q + 1)
                if q == 1:
                    dve.wait_ge(first_done, g + 1)
                else:
                    dve.wait_ge(max_done, (NR - 1) * g + q - 1)
                ps = rel_ps[q % 3][:]
                if q < len(X_RELS):
                    op = dve.scalar_tensor_tensor(out=best[:], in0=ps, scalar=c_col[:, q:q + 1], in1=best[:],
                                                  op0=ALU.add, op1=ALU.max)
                else:
                    op = dve.tensor_tensor(best[:], ps, best[:], ALU.max)
                op.then_inc(max_done, 1)

            def add_residual(g):
                odd = g[1]
                g = 2 * g[0] + g[1]
                dve.wait_ge(back_tr, g + 1)
                dve.wait_ge(xb_done, g + 1)
                after(dve, o_done, C * g)
                dve.tensor_tensor(t[:], misc_ps[:].rearrange("p (j f) -> p j f", j=C), xb[odd][:],
                                  ALU.add).then_inc(t_done, 1)
                dve.wait_ge(t_done, g + 1)
                after(dve, mean_done, C * g)
                for j in range(C):
                    dve.bn_stats(stats[:, j, :], t[:, j, :]).then_inc(stats_done, 1)

            def wait_stats(half, odd):
                g = 2 * half + odd
                dve.wait_ge(stats_done, C * (g + 1))
                after(dve, var_done, 2 * g)

            def mean_and_variance():
                for j in range(C):
                    dve.bn_aggr(mean_var[:, j, :], stats[:, j, :]).then_inc(mean_done, 1)

            def step(half, odd, early, late):
                g = 2 * half + odd
                nxt = following(half, odd)
                prev = (half, 0) if odd else (half - 1, 1)
                dve.wait_ge(sums_tr, g + 1)
                after(dve, rel_mm, NR * g)
                dve.tensor_tensor(sum_rows[:].rearrange("p (j n) -> p j n", j=C),
                                  misc_ps[:, 0:P].rearrange("p (a n) -> p a n", a=1).to_broadcast([P, C, P]),
                                  chunk_mask[:].rearrange("p (j a) -> p j a", a=1).to_broadcast([P, C, P]),
                                  ALU.mult).then_inc(sum_rows_done, 1)
                if early:
                    split_at(*nxt, 0)
                    split_at(*nxt, 1)
                if late:
                    add_residual(prev)
                if late:
                    wait_stats(*prev)
                dve.wait_ge(zt_hi_done, g + 1)
                dve.tensor_tensor(zt_lo[:], z_ps[:], zt_hi[:].bitcast(F32), ALU.subtract).then_inc(zt_lo_done, 1)
                if late:
                    mean_and_variance()
                if early:
                    split_at(*nxt, 2)
                    split_at(*nxt, 3)
                dve.wait_ge(yt_hi_done, g + 1)
                dve.tensor_tensor(yt_lo[:], y_ps[:], yt_hi[:].bitcast(F32), ALU.subtract).then_inc(yt_lo_done, 1)
                take_max(g, 1)
                take_max(g, 2)
                if early:
                    split_xt(*nxt)
                for q in range(3, NR):
                    take_max(g, q)

            graphs(dve, step)
            add_residual((GRAPHS // 2 - 1, 1))
            wait_stats(GRAPHS // 2 - 1, 1)
            mean_and_variance()

        @block.gpsimd
        def _(pool):
            def split_a(half, odd, j):
                g = 2 * half + odd
                pool.wait_ge(a_hi_done, C * g + j + 1)
                if j == 0:
                    after(pool, z_mm, g - 1)
                pool.tensor_tensor(a_lo[odd][:, j, :], a[odd][:, j, :], a_hi[odd][:, j, :].bitcast(F32),
                                   ALU.subtract).then_inc(a_lo_done, 1)

            def split_x(half, odd):
                g = 2 * half + odd
                pool.wait_ge(x_hi_done, g + 1)
                after(pool, y_mm, g - 1)
                pool.tensor_tensor(x_lo[odd][:], xs[odd][:], x_hi[odd][:].bitcast(F32),
                                   ALU.subtract).then_inc(x_lo_done, 1)

            def split_sums(half, odd):
                g = 2 * half + odd
                n = 2 * C
                pool.wait_ge(a_hi_done, C * (g + 1))
                pool.wait_ge(at_hi_done, C * (g + 1))
                after(pool, parts_done, 2 * g)
                after(pool, sums_tr, g - 1)
                pool.tensor_tensor(sums_hi[:], sums[odd][:], zeros[:], ALU.add).then_inc(sums_hi_done, 1)
                pool.wait_ge(sums_hi_done, g + 1)
                parts = sum_parts[odd][:, 0:4 * n].rearrange("p (b a n) -> p b a n", b=2, n=n)
                pool.tensor_tensor(parts[:, 0, 1, :], sums[odd][:], sums_hi[:].bitcast(F32),
                                   ALU.subtract).then_inc(parts_done, 1)
                pool.tensor_copy(parts[:, :, 0, :],
                                 sums_hi[:].bitcast(F32).rearrange("p (a n) -> p a n", a=1).to_broadcast([P, 2, n])
                                 ).then_inc(parts_done, 1)

            def add_bias(half, odd):
                g = 2 * half + odd
                pool.wait_ge(x_in[odd], 16 * (half + 1))
                after(pool, t_done, g - 1)
                pool.tensor_tensor(xb[odd][:], xs[odd][:], bias[:], ALU.add).then_inc(xb_done, 1)

            def inverse_deviation(half, odd):
                g = 2 * half + odd
                pool.wait_ge(mean_done, C * (g + 1))
                pool.tensor_tensor(neg_mean[:], zeros[:, 0:C], mean_var[:, :, 0], ALU.subtract).then_inc(var_done, 1)
                pool.tensor_tensor(var_eps[:], mean_var[:, :, 1], eps[:], ALU.add).then_inc(var_done, 1)
                pool.wait_ge(var_done, 2 * (g + 1))
                after(pool, o_done, C * g)
                pool.tensor_tensor(rstd[:], var_eps[:], neg_half[:], ALU.pow).then_inc(rstd_done, 1)
                pool.wait_ge(rstd_done, 2 * g + 1)
                pool.tensor_tensor(shift[:], neg_mean[:], rstd[:], ALU.mult).then_inc(rstd_done, 1)

            for j in range(C):
                split_a(0, 0, j)
            split_x(0, 0)
            pool.wait_ge(pads_zero, 5)
            split_sums(0, 0)
            pool.wait_ge(consts_in, 6 * 16)
            add_bias(0, 0)

            def step(half, odd, early, late):
                nxt = following(half, odd)
                prev = (half, 0) if odd else (half - 1, 1)
                if early:
                    for j in range(C - 1):
                        split_a(*nxt, j)
                if late:
                    inverse_deviation(*prev)
                if early:
                    split_a(*nxt, C - 1)
                    split_x(*nxt)
                    split_sums(*nxt)
                    add_bias(*nxt)

            graphs(pool, step)
            inverse_deviation(GRAPHS // 2 - 1, 1)

        @block.tensor
        def _(pe):
            def transpose_a(half, odd, k):
                g = 2 * half + odd
                if k == 0:
                    pe.wait_ge(a_in[odd], 16 * (half + 1))
                after(pe, at_lo_done, C * g + k - 1)
                for j in range(C):
                    op = pe.transpose(at_ps[k % 2][:, j * P:(j + 1) * P], a[odd][:, j, k * P:(k + 1) * P], ident[:])
                op.then_inc(at_tr, 1)

            def transpose_x(half, odd):
                g = 2 * half + odd
                pe.wait_ge(x_in[odd], 16 * (half + 1))
                after(pe, t_done, g - 1)
                for j in range(C):
                    op = pe.transpose(misc_ps[:, j * P:(j + 1) * P], xs[odd][:, j, :], ident[:])
                op.then_inc(xt_tr, 1)

            def transpose_back(g):
                pe.wait_ge(max_done, (NR - 1) * (g + 1))
                for j in range(C):
                    op = pe.transpose(misc_ps[:, j * P:(j + 1) * P], best[:, j * P:(j + 1) * P], ident[:])
                op.then_inc(back_tr, 1)

            def product(ps, w_parts, v_parts, start, stop):
                (wh, wl), (vh, vl) = w_parts, v_parts
                pe.matmul(ps, wh, vh, start=start, stop=False)
                pe.matmul(ps, wh, vl, start=False, stop=False)
                return pe.matmul(ps, wl, vh, start=False, stop=stop)

            pe.wait_ge(ident_in, 16)
            transpose_x(0, 0)
            for k in range(C):
                transpose_a(0, 0, k)
            pe.wait_ge(consts_in, 6 * 16)
            pe.wait_ge(edge_lhs_done, len(OUTER))
            for n, r in enumerate(OUTER):
                pe.matmul(rel_ps[0][:, n * OUT:(n + 1) * OUT], edge_lhs[:, n, :], w_edge[:, r, :],
                          start=True, stop=True)
            for n, r in enumerate(X_RELS):
                op = pe.matmul(rel_ps[1][:, n:n + 1], w_edge[:, r, :], edges[:, r:r + 1], start=True, stop=True)
            op.then_inc(c_mm, 1)

            def step(half, odd, early, late):
                g = 2 * half + odd
                nxt = following(half, odd)
                pe.wait_ge(x_lo_done, g + 1)
                after(pe, zt_lo_done, g)
                for j in range(C):
                    pe.wait_ge(a_lo_done, C * g + j + 1)
                    op = product(z_ps[:], (x_hi[odd][:, j, :], x_lo[odd][:, j, :]),
                                 (a_hi[odd][:, j, :], a_lo[odd][:, j, :]), j == 0, j == C - 1)
                    if j == C - 1:
                        op.then_inc(z_mm, 1)
                    if j == 0:
                        pe.wait_ge(parts_done, 2 * (g + 1))
                        pe.wait_ge(xt_lo_done, g + 1)
                        pe.transpose(misc_ps[:, 0:P], sum_parts[odd][:], ident[:]).then_inc(sums_tr, 1)
                    if early and j % 2:
                        transpose_a(*nxt, j // 2)
                pe.wait_ge(sum_rows_done, g + 1)
                if late:
                    transpose_back(g - 1)
                after(pe, yt_lo_done, g)
                for k in range(C):
                    pe.wait_ge(at_lo_done, C * g + k + 1)
                    op = product(y_ps[:], (x_hi[odd][:, k, :], x_lo[odd][:, k, :]),
                                 (at_hi[odd][:, k, :], at_lo[odd][:, k, :]), k == 0, k == C - 1)
                    if k == C - 1:
                        op.then_inc(y_mm, 1)
                    if early and k % 2:
                        transpose_a(*nxt, 2 + k // 2)
                if not late:
                    pe.wait_ge(w_lo_done, 1)
                    pe.wait_ge(c_done, 2)
                for q, r in enumerate(RELS):
                    if q == 0:
                        after(pe, max_done, (NR - 1) * g)
                    elif q == 3:
                        pe.wait_ge(first_done, g + 1)
                    elif q > 3:
                        pe.wait_ge(max_done, (NR - 1) * g + q - 3)
                    if r in X_RELS:
                        v_parts = (xt_hi[odd][:], xt_lo[odd][:])
                    elif r in Z_RELS:
                        pe.wait_ge(zt_lo_done, g + 1)
                        v_parts = (zt_hi[:], zt_lo[:])
                    else:
                        pe.wait_ge(yt_lo_done, g + 1)
                        v_parts = (yt_hi[:], yt_lo[:])
                    ps = rel_ps[q % 3][:]
                    op = product(ps, (w_hi[:, r, :], w_lo[:, r, :]), v_parts, True, r in X_RELS)
                    if r in OUTER:
                        op = pe.matmul(ps, c_rows[:, OUTER.index(r), :], sum_rows[:], start=False, stop=True)
                    op.then_inc(rel_mm, 1)
                    if early and q == 1:
                        transpose_x(*nxt)

            graphs(pe, step)
            transpose_back(GRAPHS - 1)


def kernel(x, adj, L0_gnn_W, L0_gnn_W_edges, L0_gnn_b):
    import numpy as np
    import concourse.bacc as bacc
    from concourse.bass_utils import run_bass_kernel_spmd

    row = np.arange(P)
    used = row < ROWS
    arrays = {
        "x": x, "adj": adj, "w": L0_gnn_W, "w_edges": L0_gnn_W_edges, "b": L0_gnn_b,
        "ident": np.eye(P, dtype=np.float32),
        "chunk": (used[:, None] & (row[:, None] % 4 == np.arange(4))).astype(np.float32),
        "lo_rows": -(used & (row // 8 == 2)).astype(np.float32)[:, None],
        "side": np.broadcast_to(used & (row // 4 % 2 == np.arange(2)[:, None]), (16, 2, P)).astype(np.float32),
    }
    arrays = {f"in_{k}_dram": np.ascontiguousarray(v) for k, v in arrays.items()}
    nc = bacc.Bacc("TRN2", target_bir_lowering=False, num_devices=1)
    args = [nc.dram_tensor(k, v.shape, mybir.dt.from_np(v.dtype), kind="ExternalInput").ap()
            for k, v in arrays.items()]
    out = nc.dram_tensor("out_dram", x.shape, F32, kind="ExternalOutput").ap()
    graph_layer(nc, *args, out)
    r = run_bass_kernel_spmd(nc, [arrays], core_ids=[0])
    return r.results[0]["out_dram"]
```

```python
from contextlib import ExitStack

import concourse.bass as bass
from concourse import mybir


F32 = mybir.dt.float32
F32R = mybir.dt.float32r
ACT = mybir.ActivationFunctionType
ALU = mybir.AluOpType

P = 128
ROWS = 24
EPS = 1e-5
X_RELS, Z_RELS, Y_RELS = (2, 5, 6), (3, 4), (0, 1)
RELS = X_RELS + Z_RELS + Y_RELS
OUTER = Y_RELS + Z_RELS
Q = 32
ON_VECTOR, ON_GPSIMD, EXACT = (0,), (1,), (2, 3)


def graph_layer(nc, x, adj, W, W_edges, b, tables_d, out):
    GRAPHS, NODES, FEAT = x.shape
    N_REL, K_ALL, OUT = W.shape
    EDGE = K_ALL - FEAT
    C = NODES // P
    NR = len(RELS)
    assert FEAT == P and OUT == P and NODES == 512 and GRAPHS % 2 == 0

    x_d = x.rearrange("g (q k c) f -> g q c k f", q=4, c=Q)
    adj_d = adj.rearrange("g (q k c) m -> g q c k m", q=4, c=Q)
    out_d = out.rearrange("g (q k c) f -> g q c k f", q=4, c=Q)
    bias_d = b.rearrange("(q k c) o -> q c k o", q=4, c=Q)
    blocks_d = adj.rearrange("g (i r) (q m) -> g q r i m", r=Q, q=4)

    ctx = ExitStack()
    with ctx:
        def sb(name, shape, dt=F32):
            return ctx.enter_context(nc.sbuf_tensor(name, shape, dt))

        def bank(name):
            return ctx.enter_context(nc.psum_tensor(name, [P, 512], F32))

        def sem(name):
            return ctx.enter_context(nc.semaphore(name))

        tables = sb("tables", [P, 3 * P + C + 1])
        ident = tables[:, 0:P]
        side_mask = tables[0:EDGE, P:3 * P].rearrange("p (s n) -> p s n", s=2)
        chunk_mask = tables[:, 3 * P:3 * P + C]
        lo_rows = tables[:, 3 * P + C:3 * P + C + 1]
        w = sb("w", [P, N_REL, OUT])
        w_hi = sb("w_hi", [P, N_REL, OUT], F32R)
        w_lo = sb("w_lo", [P, N_REL, OUT], F32R)
        w_edge = sb("w_edge", [EDGE, N_REL, OUT])
        edges = sb("edges", [EDGE, N_REL])
        edge_lhs = sb("edge_lhs", [EDGE, len(OUTER), P])
        c_hi = sb("c_hi", [P, len(OUTER), OUT], F32R)
        c_rows = sb("c_rows", [P, len(OUTER), OUT], F32R)
        c_col = sb("c_col", [P, len(X_RELS)])
        bias = sb("bias", [P, C, OUT])
        eps = sb("eps", [P, C])
        neg_half = sb("neg_half", [P, C])
        zeros = sb("zeros", [P, 2 * C])

        blocks = [sb(f"blocks{n}", [P, NODES // Q, P]) for n in range(2)]
        at = [sb(f"at{n}", [P, C, NODES]) for n in range(2)]
        a = [sb(f"a{n}", [P, C, NODES]) for n in range(2)]
        a_hi = [sb(f"a_hi{n}", [P, C, NODES], F32R) for n in range(2)]
        a_lo = [sb(f"a_lo{n}", [P, C, NODES], F32R) for n in range(2)]
        at_hi = [sb(f"at_hi{n}", [P, C, NODES], F32R) for n in range(2)]
        at_lo = [sb(f"at_lo{n}", [P, C, NODES], F32R) for n in range(2)]
        xs = [sb(f"xs{n}", [P, C, FEAT]) for n in range(2)]
        x_hi = [sb(f"x_hi{n}", [P, C, FEAT], F32R) for n in range(2)]
        x_lo = [sb(f"x_lo{n}", [P, C, FEAT], F32R) for n in range(2)]
        xt_hi = [sb(f"xt_hi{n}", [P, NODES], F32R) for n in range(2)]
        xt_lo = [sb(f"xt_lo{n}", [P, NODES], F32R) for n in range(2)]
        xb = [sb(f"xb{n}", [P, C, FEAT]) for n in range(2)]
        sums = [sb(f"sums{n}", [P, 2 * C]) for n in range(2)]
        sum_parts = [sb(f"sum_parts{n}", [P, P]) for n in range(2)]
        o = [sb(f"o{n}", [P, C, OUT]) for n in range(2)]
        sums_hi = sb("sums_hi", [P, 2 * C], F32R)
        sum_rows = sb("sum_rows", [P, NODES], F32R)
        zt_hi = sb("zt_hi", [P, NODES], F32R)
        zt_lo = sb("zt_lo", [P, NODES], F32R)
        yt_hi = sb("yt_hi", [P, NODES], F32R)
        yt_lo = sb("yt_lo", [P, NODES], F32R)
        best = sb("best", [P, NODES])
        best_by_chunk = sb("best_by_chunk", [P, NODES])
        t = sb("t", [P, C, OUT])
        stats = sb("stats", [P, C, 6])
        mean_var = sb("mean_var", [P, C, 2])
        var_eps = sb("var_eps", [P, C])
        rstd = sb("rstd", [P, C])
        neg_mean = sb("neg_mean", [P, C])
        shift = sb("shift", [P, C])

        z_ps, y_ps = bank("z_ps"), bank("y_ps")
        rel_ps = [bank(f"rel_ps{n}") for n in range(4)]
        xt_ps = bank("xt_ps")
        misc_ps = bank("misc_ps")

        tables_in = sem("tables_in")
        w_in = sem("w_in")
        bias_in = sem("bias_in")
        edges_in = sem("edges_in")
        x_in = [sem("x_in0"), sem("x_in1")]
        a_in = [sem("a_in0"), sem("a_in1")]
        blocks_in = [sem("blocks_in0"), sem("blocks_in1")]
        stored = [sem("stored0"), sem("stored1")]
        w_hi_done = sem("w_hi_done")
        w_lo_done = sem("w_lo_done")
        pads_zero = sem("pads_zero")
        edge_lhs_done = sem("edge_lhs_done")
        c_mm = sem("c_mm")
        c_hi_done = sem("c_hi_done")
        c_done = sem("c_done")
        a_hi_done = sem("a_hi_done")
        a_lo_done = sem("a_lo_done")
        at_tr = sem("at_tr")
        at_hi_done = sem("at_hi_done")
        at_lo_v = sem("at_lo_v")
        at_lo_g = sem("at_lo_g")
        x_hi_done = sem("x_hi_done")
        x_lo_done = sem("x_lo_done")
        xb_done = sem("xb_done")
        xt_tr = sem("xt_tr")
        xt_hi_done = sem("xt_hi_done")
        xt_lo_done = sem("xt_lo_done")
        sums_hi_done = sem("sums_hi_done")
        parts_done = sem("parts_done")
        sums_tr = sem("sums_tr")
        sum_rows_done = sem("sum_rows_done")
        z_mm = sem("z_mm")
        zt_hi_done = sem("zt_hi_done")
        zt_lo_done = sem("zt_lo_done")
        y_mm = sem("y_mm")
        yt_hi_done = sem("yt_hi_done")
        yt_lo_done = sem("yt_lo_done")
        rel_mm = sem("rel_mm")
        first_done = sem("first_done")
        max_done = sem("max_done")
        back_tr = sem("back_tr")
        t_done = sem("t_done")
        stats_done = sem("stats_done")
        mean_done = sem("mean_done")
        var_done = sem("var_done")
        rstd_done = sem("rstd_done")
        o_done = sem("o_done")

        block = ctx.enter_context(nc.Block())

        def after(eng, s, value):
            if not isinstance(value, int) or value > 0:
                eng.wait_ge(s, value)

        def graphs(eng, step):
            step(0, 0, True, False)
            with eng.Fori(0, GRAPHS // 2 - 1) as h:
                step(h, 1, True, True)
                step(h + 1, 0, True, True)
            step(GRAPHS // 2 - 1, 1, False, True)

        def following(half, odd):
            return (half + 1, 0) if odd else (half, 1)

        @block.sync
        def _(sp):
            def four(dst, src, s):
                for q in range(4):
                    sp.dma_start(dst[q * Q:(q + 1) * Q], src[q]).then_inc(s, 16)

            def load(half, odd, graph, graph_2=False):
                after(sp, a_hi_done, C * (graph - 1))
                after(sp, a_lo_done, C * (graph - 2))
                if graph_2:
                    sp.wait_ge(z_mm, 1)
                four(a[odd], adj_d[graph], a_in[odd])
                after(sp, at_tr, C * (graph - 1))
                four(blocks[odd], blocks_d[graph], blocks_in[odd])
                after(sp, x_lo_done, graph - 2)
                after(sp, xt_tr, graph - 1)
                after(sp, xb_done, graph - 1)
                after(sp, y_mm, graph - 1)
                four(xs[odd], x_d[graph], x_in[odd])

            def store(half, odd, graph):
                after(sp, o_done, C * (graph + 1))
                for q in range(4):
                    sp.dma_start(out_d[graph][q], o[odd][q * Q:(q + 1) * Q]).then_inc(stored[odd], 16)

            four(xs[0], x_d[0], x_in[0])
            four(a[0], adj_d[0], a_in[0])
            four(blocks[0], blocks_d[0], blocks_in[0])
            load(0, 1, 1)
            load(1, 0, 2, graph_2=True)
            with sp.Fori(0, GRAPHS // 2 - 2) as h:
                load(h + 1, 1, 2 * h + 3)
                store(h, 0, 2 * h)
                load(h + 2, 0, 2 * h + 4)
                store(h, 1, 2 * h + 1)
            last = GRAPHS // 2 - 1
            load(last, 1, 2 * last + 1)
            for graph in range(2 * last - 2, GRAPHS):
                store(graph // 2, graph % 2, graph)
            for s in stored:
                sp.wait_ge(s, 64 * (GRAPHS // 2))

        @block.scalar
        def _(act):
            def split_a(half, odd, j):
                g = 2 * half + odd
                if j == 0:
                    act.wait_ge(a_in[odd], 64 * (half + 1))
                    after(act, z_mm, g - 1)
                    after(act, parts_done, 2 * (g - 1))
                act.activation(a_hi[odd][:, j, :], a[odd][:, j, :], ACT.Copy,
                               accum_out=sums[odd][:, j:j + 1]).then_inc(a_hi_done, 1)

            def split_at(half, odd, k):
                g = 2 * half + odd
                act.wait_ge(at_tr, C * g + k + 1)
                if k == 0:
                    after(act, y_mm, g - 1)
                    after(act, parts_done, 2 * (g - 1))
                act.activation(at_hi[odd][:, k, :], at[odd][:, k, :], ACT.Copy,
                               accum_out=sums[odd][:, C + k:C + k + 1]).then_inc(at_hi_done, 1)

            def split_xt(half, odd):
                act.wait_ge(xt_tr, 2 * half + odd + 1)
                act.activation(xt_hi[odd][:], xt_ps[:], ACT.Copy).then_inc(xt_hi_done, 1)

            def round_x(half, odd):
                act.wait_ge(x_in[odd], 64 * (half + 1))
                after(act, y_mm, 2 * half + odd - 1)
                act.activation(x_hi[odd][:], xs[odd][:], ACT.Copy).then_inc(x_hi_done, 1)

            def normalize(half, odd):
                g = 2 * half + odd
                act.wait_ge(rstd_done, 2 * (g + 1))
                after(act, stored[odd], 64 * half)
                for j in range(C):
                    act.activation(o[odd][:, j, :], t[:, j, :], ACT.Identity, bias=shift[:, j:j + 1],
                                   scale=rstd[:, j:j + 1]).then_inc(o_done, 1)

            act.dma_start(w[:], W[:, 0:FEAT, :].rearrange("r f o -> f r o")).then_inc(w_in, 16)
            for q in range(4):
                act.dma_start(bias[q * Q:(q + 1) * Q], bias_d[q]).then_inc(bias_in, 16)
            split_xt(0, 0)
            for j in range(C):
                split_a(0, 0, j)
            act.wait_ge(w_in, 16)
            act.activation(w_hi[:], w[:], ACT.Copy).then_inc(w_hi_done, 1)
            for k in range(C):
                split_at(0, 0, k)

            def split_z(g):
                act.wait_ge(z_mm, g + 1)
                act.activation(zt_hi[:], z_ps[:], ACT.Copy).then_inc(zt_hi_done, 1)

            def split_y(g):
                act.wait_ge(y_mm, g + 1)
                act.activation(yt_hi[:], y_ps[:], ACT.Copy).then_inc(yt_hi_done, 1)

            def start_max(g):
                act.wait_ge(rel_mm, NR * g + 1)
                act.activation(best[:], rel_ps[0][:], ACT.Identity, bias=c_col[:, 0:1]).then_inc(first_done, 1)

            def step(half, odd, early, late):
                g = 2 * half + odd
                nxt = following(half, odd)
                prev = (half, 0) if odd else (half - 1, 1)
                if not late:
                    split_z(g)
                    split_y(g)
                    act.wait_ge(c_done, 2)
                    start_max(g)
                    round_x(*nxt)
                    for k in range(C):
                        split_a(*nxt, k)
                    split_xt(*nxt)
                    for k in range(C):
                        split_at(*nxt, k)
                    return
                if early:
                    split_a(*nxt, 0)
                    round_x(*nxt)
                    split_a(*nxt, 1)
                    split_a(*nxt, 2)
                    split_at(*nxt, 0)
                split_z(g)
                if early:
                    split_a(*nxt, 3)
                    split_at(*nxt, 1)
                    split_at(*nxt, 2)
                split_y(g)
                start_max(g)
                if early:
                    split_xt(*nxt)
                    split_at(*nxt, 3)
                normalize(*prev)

            graphs(act, step)
            normalize(GRAPHS // 2 - 1, 1)

        @block.vector
        def _(dve):
            def transpose_a(half, odd, k):
                g = 2 * half + odd
                if k == 0:
                    dve.wait_ge(blocks_in[odd], 64 * (half + 1))
                    after(dve, at_hi_done, C * (g - 1))
                    after(dve, at_lo_g, len(ON_GPSIMD) * (g - 2))
                    after(dve, at_lo_v, len(ON_VECTOR) * (g - 2))
                    after(dve, y_mm, g - 1)
                dve.transpose(at[odd][:, k, :], blocks[odd][:, :, k * Q:(k + 1) * Q]).then_inc(at_tr, 1)

            def split_at(half, odd, k):
                g = 2 * half + odd
                dve.wait_ge(at_hi_done, C * g + k + 1)
                after(dve, y_mm, g - 1)
                dve.tensor_tensor(at_lo[odd][:, k, :], at[odd][:, k, :], at_hi[odd][:, k, :].bitcast(F32),
                                  ALU.subtract).then_inc(at_lo_v, 1)

            def split_xt(half, odd):
                dve.wait_ge(xt_hi_done, 2 * half + odd + 1)
                dve.tensor_tensor(xt_lo[odd][:], xt_ps[:], xt_hi[odd][:].bitcast(F32),
                                  ALU.subtract).then_inc(xt_lo_done, 1)

            for n in range(2):
                dve.memset(sum_parts[n][:], 0.0).then_inc(pads_zero, 1)
            dve.memset(eps[:], EPS).then_inc(pads_zero, 1)
            dve.memset(neg_half[:], -0.5).then_inc(pads_zero, 1)
            dve.memset(zeros[:], 0.0).then_inc(pads_zero, 1)
            dve.wait_ge(tables_in, 16)
            dve.wait_ge(edges_in, 2 * 16)
            for n, r in enumerate(OUTER):
                dve.tensor_scalar(edge_lhs[:, n, :], side_mask[:, 0 if r in Y_RELS else 1, :], edges[:, r:r + 1],
                                  None, ALU.mult).then_inc(edge_lhs_done, 1)
            split_xt(0, 0)
            dve.wait_ge(c_mm, 1)
            dve.tensor_copy(c_hi[:], rel_ps[0][:]).then_inc(c_hi_done, 1)
            dve.tensor_copy(c_col[:], rel_ps[1][:, 0:len(X_RELS)]).then_inc(c_done, 1)
            dve.wait_ge(c_hi_done, 1)
            dve.scalar_tensor_tensor(out=c_rows[:], in0=c_hi[:].bitcast(F32), scalar=lo_rows,
                                     in1=rel_ps[0][:].rearrange("p (r o) -> p r o", o=OUT),
                                     op0=ALU.mult, op1=ALU.add).then_inc(c_done, 1)
            for k in range(C):
                transpose_a(0, 0, k)
            dve.wait_ge(w_hi_done, 1)
            dve.tensor_tensor(w_lo[:], w[:], w_hi[:].bitcast(F32), ALU.subtract).then_inc(w_lo_done, 1)

            def take_max(g, q):
                dve.wait_ge(rel_mm, NR * g + q + 1)
                if q == 1:
                    dve.wait_ge(first_done, g + 1)
                else:
                    dve.wait_ge(max_done, (NR - 1) * g + q - 1)
                ps = rel_ps[q % 4][:]
                if q < len(X_RELS):
                    op = dve.scalar_tensor_tensor(out=best[:], in0=ps, scalar=c_col[:, q:q + 1], in1=best[:],
                                                  op0=ALU.add, op1=ALU.max)
                elif q < NR - 1:
                    op = dve.tensor_tensor(best[:], ps, best[:], ALU.max)
                else:
                    after(dve, back_tr, g)
                    nodes = "p (q k c) -> p q k c"
                    op = dve.tensor_tensor(best_by_chunk[:].rearrange("p (k q c) -> p q k c", k=C, q=4),
                                           ps.rearrange(nodes, q=4, k=C), best[:].rearrange(nodes, q=4, k=C),
                                           ALU.max)
                op.then_inc(max_done, 1)

            def add_residual(g):
                odd = g[1]
                g = 2 * g[0] + g[1]
                dve.wait_ge(back_tr, g + 1)
                dve.wait_ge(xb_done, g + 1)
                after(dve, o_done, C * g)
                dve.tensor_tensor(t[:], misc_ps[:].rearrange("p (j f) -> p j f", j=C), xb[odd][:],
                                  ALU.add).then_inc(t_done, 1)
                dve.wait_ge(t_done, g + 1)
                after(dve, mean_done, C * g)
                for j in range(C):
                    dve.bn_stats(stats[:, j, :], t[:, j, :]).then_inc(stats_done, 1)

            def wait_stats(half, odd):
                g = 2 * half + odd
                dve.wait_ge(stats_done, C * (g + 1))
                after(dve, var_done, 2 * g)

            def mean_and_variance():
                for j in range(C):
                    dve.bn_aggr(mean_var[:, j, :], stats[:, j, :]).then_inc(mean_done, 1)

            def spread_sums(g):
                dve.wait_ge(sums_tr, g + 1)
                after(dve, rel_mm, NR * g)
                by_chunk = "p (q k c) -> p k q c"
                dve.tensor_tensor(sum_rows[:].rearrange(by_chunk, q=4, k=C),
                                  misc_ps[:, 0:P].rearrange("p (a q c) -> p a q c", a=1, q=4)
                                  .to_broadcast([P, C, 4, Q]),
                                  chunk_mask.rearrange("p (k a b) -> p k a b", a=1, b=1)
                                  .to_broadcast([P, C, 4, Q]), ALU.mult).then_inc(sum_rows_done, 1)

            def split_z(g):
                dve.wait_ge(zt_hi_done, g + 1)
                dve.tensor_tensor(zt_lo[:], z_ps[:], zt_hi[:].bitcast(F32), ALU.subtract).then_inc(zt_lo_done, 1)

            def split_y(g):
                dve.wait_ge(yt_hi_done, g + 1)
                dve.tensor_tensor(yt_lo[:], y_ps[:], yt_hi[:].bitcast(F32), ALU.subtract).then_inc(yt_lo_done, 1)

            def step(half, odd, early, late):
                g = 2 * half + odd
                nxt = following(half, odd)
                prev = (half, 0) if odd else (half - 1, 1)
                if not late:
                    split_z(g)
                    split_y(g)
                    take_max(g, 1)
                    spread_sums(g)
                    take_max(g, 2)
                    for k in range(C):
                        take_max(g, 3 + k)
                        transpose_a(*nxt, k)
                    for k in ON_VECTOR:
                        split_at(*nxt, k)
                    split_xt(*nxt)
                    return
                spread_sums(g)
                if early:
                    transpose_a(*nxt, 0)
                    transpose_a(*nxt, 1)
                add_residual(prev)
                wait_stats(*prev)
                split_z(g)
                mean_and_variance()
                if early:
                    transpose_a(*nxt, 2)
                    transpose_a(*nxt, 3)
                    for k in ON_VECTOR:
                        split_at(*nxt, k)
                split_y(g)
                take_max(g, 1)
                take_max(g, 2)
                if early:
                    split_xt(*nxt)
                for q in range(3, NR):
                    take_max(g, q)

            graphs(dve, step)
            add_residual((GRAPHS // 2 - 1, 1))
            wait_stats(GRAPHS // 2 - 1, 1)
            mean_and_variance()

        @block.gpsimd
        def _(pool):
            def split_a(half, odd, j):
                g = 2 * half + odd
                pool.wait_ge(a_hi_done, C * g + j + 1)
                if j == 0:
                    after(pool, z_mm, g - 1)
                pool.tensor_tensor(a_lo[odd][:, j, :], a[odd][:, j, :], a_hi[odd][:, j, :].bitcast(F32),
                                   ALU.subtract).then_inc(a_lo_done, 1)

            def split_at(half, odd, k):
                g = 2 * half + odd
                pool.wait_ge(at_hi_done, C * g + k + 1)
                after(pool, y_mm, g - 1)
                pool.tensor_tensor(at_lo[odd][:, k, :], at[odd][:, k, :], at_hi[odd][:, k, :].bitcast(F32),
                                   ALU.subtract).then_inc(at_lo_g, 1)

            def split_x(half, odd):
                g = 2 * half + odd
                pool.wait_ge(x_hi_done, g)
                after(pool, y_mm, g - 1)
                pool.tensor_tensor(x_lo[odd][:], xs[odd][:], x_hi[odd][:].bitcast(F32),
                                   ALU.subtract).then_inc(x_lo_done, 1)

            def split_sums(half, odd):
                g = 2 * half + odd
                n = 2 * C
                pool.wait_ge(a_hi_done, C * (g + 1))
                pool.wait_ge(at_hi_done, C * (g + 1))
                after(pool, parts_done, 2 * g)
                after(pool, sums_tr, g - 1)
                pool.tensor_tensor(sums_hi[:], sums[odd][:], zeros[:], ALU.add).then_inc(sums_hi_done, 1)
                pool.wait_ge(sums_hi_done, g + 1)
                parts = sum_parts[odd][:, 0:4 * n].rearrange("p (b a n) -> p b a n", b=2, n=n)
                pool.tensor_tensor(parts[:, 0, 1, :], sums[odd][:], sums_hi[:].bitcast(F32),
                                   ALU.subtract).then_inc(parts_done, 1)
                pool.tensor_copy(parts[:, :, 0, :],
                                 sums_hi[:].bitcast(F32).rearrange("p (a n) -> p a n", a=1).to_broadcast([P, 2, n])
                                 ).then_inc(parts_done, 1)

            def add_bias(half, odd):
                g = 2 * half + odd
                pool.wait_ge(x_in[odd], 64 * (half + 1))
                after(pool, t_done, g - 1)
                pool.tensor_tensor(xb[odd][:], xs[odd][:], bias[:], ALU.add).then_inc(xb_done, 1)

            def inverse_deviation(half, odd):
                g = 2 * half + odd
                pool.wait_ge(mean_done, C * (g + 1))
                pool.tensor_tensor(neg_mean[:], zeros[:, 0:C], mean_var[:, :, 0], ALU.subtract).then_inc(var_done, 1)
                pool.tensor_tensor(var_eps[:], mean_var[:, :, 1], eps[:], ALU.add).then_inc(var_done, 1)
                pool.wait_ge(var_done, 2 * (g + 1))
                after(pool, o_done, C * g)
                pool.tensor_tensor(rstd[:], var_eps[:], neg_half[:], ALU.pow).then_inc(rstd_done, 1)
                pool.wait_ge(rstd_done, 2 * g + 1)
                pool.tensor_tensor(shift[:], neg_mean[:], rstd[:], ALU.mult).then_inc(rstd_done, 1)

            pool.dma_start(tables[:], tables_d).then_inc(tables_in, 16)
            with nc.allow_non_contiguous_dma(reason="112 numbers"):
                pool.dma_start(edges[:], W_edges.rearrange("r d -> d r")).then_inc(edges_in, 16)
            pool.dma_start(w_edge[:], W[:, FEAT:K_ALL, :].rearrange("r d o -> d r o")).then_inc(edges_in, 16)
            pool.wait_ge(pads_zero, 5)
            split_sums(0, 0)
            pool.wait_ge(bias_in, 4 * 16)
            add_bias(0, 0)

            def step(half, odd, early, late):
                nxt = following(half, odd)
                prev = (half, 0) if odd else (half - 1, 1)
                if early:
                    for j in range(C - 1):
                        split_a(*nxt, j)
                if late:
                    inverse_deviation(*prev)
                if early:
                    split_a(*nxt, C - 1)
                    split_x(*nxt)
                    for k in ON_GPSIMD:
                        split_at(*nxt, k)
                    split_sums(*nxt)
                    add_bias(*nxt)

            graphs(pool, step)
            inverse_deviation(GRAPHS // 2 - 1, 1)

        @block.tensor
        def _(pe):
            def transpose_x(half, odd):
                g = 2 * half + odd
                pe.wait_ge(x_in[odd], 64 * (half + 1))
                after(pe, xt_lo_done, g)
                for k in range(C):
                    op = pe.transpose(xt_ps[:].rearrange("p (q k c) -> p k q c", q=4, k=C)[:, k], xs[odd][:, k, :],
                                      ident)
                op.then_inc(xt_tr, 1)

            def transpose_back(g):
                pe.wait_ge(max_done, (NR - 1) * (g + 1))
                for j in range(C):
                    op = pe.transpose(misc_ps[:, j * P:(j + 1) * P],
                                      best_by_chunk[:, j * P:(j + 1) * P], ident)
                op.then_inc(back_tr, 1)

            def transpose_sums(half, odd):
                g = 2 * half + odd
                pe.wait_ge(parts_done, 2 * (g + 1))
                after(pe, t_done, g - 1)
                pe.transpose(misc_ps[:, 0:P], sum_parts[odd][:], ident).then_inc(sums_tr, 1)

            def product(ps, w_parts, v_parts, start, stop):
                (wh, wl), (vh, vl) = w_parts, v_parts
                pe.matmul(ps, wh, vh, start=start, stop=False)
                pe.matmul(ps, wh, vl, start=False, stop=False)
                return pe.matmul(ps, wl, vh, start=False, stop=stop)

            def constants():
                pe.wait_ge(edge_lhs_done, len(OUTER))
                for n, r in enumerate(OUTER):
                    pe.matmul(rel_ps[0][:, n * OUT:(n + 1) * OUT], edge_lhs[:, n, :], w_edge[:, r, :],
                              start=True, stop=True)
                for n, r in enumerate(X_RELS):
                    op = pe.matmul(rel_ps[1][:, n:n + 1], w_edge[:, r, :], edges[:, r:r + 1], start=True, stop=True)
                op.then_inc(c_mm, 1)

            pe.wait_ge(tables_in, 16)
            transpose_x(0, 0)
            constants()
            def step(half, odd, early, late):
                g = 2 * half + odd
                nxt = following(half, odd)
                if late:
                    pe.wait_ge(x_lo_done, g)
                else:
                    pe.wait_ge(a_in[odd], 64)
                after(pe, zt_lo_done, g)
                for j in range(C):
                    first, last = j == 0, j == C - 1
                    if late:
                        pe.wait_ge(a_lo_done, C * (g - 1) + j + 1)
                        op = product(z_ps[:], (x_hi[odd][:, j, :], x_lo[odd][:, j, :]),
                                     (a_hi[odd][:, j, :], a_lo[odd][:, j, :]), first, last)
                    else:
                        op = pe.matmul(z_ps[:], xs[odd][:, j, :], a[odd][:, j, :], start=first, stop=last)
                    if j == C - 1:
                        op.then_inc(z_mm, 1)
                    if j == 0 and late:
                        transpose_sums(half, odd)
                if late:
                    pe.wait_ge(sum_rows_done, g + 1)
                    transpose_back(g - 1)
                after(pe, yt_lo_done, g)
                for k in range(C):
                    first, last = k == 0, k == C - 1
                    if k in EXACT or not late:
                        pe.wait_ge(at_tr, C * g + k + 1)
                        op = pe.matmul(y_ps[:], xs[odd][:, k, :], at[odd][:, k, :], start=first, stop=last)
                    else:
                        if k in ON_VECTOR:
                            pe.wait_ge(at_lo_v, len(ON_VECTOR) * (g - 1) + ON_VECTOR.index(k) + 1)
                        else:
                            pe.wait_ge(at_lo_g, len(ON_GPSIMD) * (g - 1) + ON_GPSIMD.index(k) + 1)
                        op = product(y_ps[:], (x_hi[odd][:, k, :], x_lo[odd][:, k, :]),
                                     (at_hi[odd][:, k, :], at_lo[odd][:, k, :]), first, last)
                    if k == C - 1:
                        op.then_inc(y_mm, 1)
                if not late:
                    pe.wait_ge(w_lo_done, 1)
                    pe.wait_ge(c_done, 2)
                for q, r in enumerate(RELS):
                    if q == 0:
                        after(pe, max_done, (NR - 1) * g)
                    elif q == 4:
                        pe.wait_ge(first_done, g + 1)
                    elif q > 4:
                        pe.wait_ge(max_done, (NR - 1) * g + q - 4)
                    if q == 0:
                        pe.wait_ge(xt_lo_done, g + 1)
                    if r in X_RELS:
                        v_parts = (xt_hi[odd][:], xt_lo[odd][:])
                    elif r in Z_RELS:
                        pe.wait_ge(zt_lo_done, g + 1)
                        pe.wait_ge(sum_rows_done, g + 1)
                        v_parts = (zt_hi[:], zt_lo[:])
                    else:
                        pe.wait_ge(yt_lo_done, g + 1)
                        v_parts = (yt_hi[:], yt_lo[:])
                    ps = rel_ps[q % 4][:]
                    op = product(ps, (w_hi[:, r, :], w_lo[:, r, :]), v_parts, True, r in X_RELS)
                    if r in OUTER:
                        op = pe.matmul(ps, c_rows[:, OUTER.index(r), :], sum_rows[:], start=False, stop=True)
                    op.then_inc(rel_mm, 1)
                    if q == 1 and not late:
                        transpose_sums(half, odd)
                    if early and q == 1:
                        transpose_x(*nxt)

            graphs(pe, step)
            transpose_back(GRAPHS - 1)


def kernel(x, adj, L0_gnn_W, L0_gnn_W_edges, L0_gnn_b):
    import numpy as np
    import concourse.bacc as bacc
    from concourse.bass_utils import run_bass_kernel_spmd

    row = np.arange(P)
    used = row < ROWS
    sides = np.broadcast_to((used & (row // 4 % 2 == np.arange(2)[:, None])).reshape(1, 2 * P), (P, 2 * P))
    chunks = used[:, None] & (row[:, None] % 4 == np.arange(4))
    lo_rows = -1.0 * (used & (row // 8 == 2))[:, None]
    arrays = {
        "x": x, "adj": adj, "w": L0_gnn_W, "w_edges": L0_gnn_W_edges, "b": L0_gnn_b,
        "tables": np.concatenate([np.eye(P), sides, chunks, lo_rows], axis=1, dtype=np.float32),
    }
    arrays = {f"in_{k}_dram": np.ascontiguousarray(v) for k, v in arrays.items()}
    nc = bacc.Bacc("TRN2", target_bir_lowering=False, num_devices=1)
    args = [nc.dram_tensor(k, v.shape, mybir.dt.from_np(v.dtype), kind="ExternalInput").ap()
            for k, v in arrays.items()]
    out = nc.dram_tensor("out_dram", x.shape, F32, kind="ExternalOutput").ap()
    graph_layer(nc, *args, out)
    r = run_bass_kernel_spmd(nc, [arrays], core_ids=[0])
    return r.results[0]["out_dram"]
```

```python
from contextlib import ExitStack

import concourse.bass as bass
from concourse import mybir


F32 = mybir.dt.float32
F32R = mybir.dt.float32r
ACT = mybir.ActivationFunctionType
ALU = mybir.AluOpType

P = 128
ROWS = 24
EPS = 1e-5
X_RELS, Z_RELS, Y_RELS = (2, 5, 6), (3, 4), (0, 1)
RELS = X_RELS + Z_RELS + Y_RELS
OUTER = Y_RELS + Z_RELS
Q = 32
ON_VECTOR, ON_GPSIMD = (0, 1), (2, 3)
LAST_ON_VECTOR, LAST_ON_SCALAR = (0, 1), (2, 3)


def graph_layer(nc, x, adj, W, W_edges, b, tables_d, out):
    GRAPHS, NODES, FEAT = x.shape
    N_REL, K_ALL, OUT = W.shape
    EDGE = K_ALL - FEAT
    C = NODES // P
    NR = len(RELS)
    assert FEAT == P and OUT == P and NODES == 512 and GRAPHS % 2 == 0

    x_d = x.rearrange("g (q k c) f -> g q c k f", q=4, c=Q)
    adj_d = adj.rearrange("g (q k c) m -> g q c k m", q=4, c=Q)
    out_d = out.rearrange("g (q k c) f -> g q c k f", q=4, c=Q)
    bias_d = b.rearrange("(q k c) o -> q c k o", q=4, c=Q)
    blocks_d = adj.rearrange("g (i r) (q m) -> g q r i m", r=Q, q=4)

    ctx = ExitStack()
    with ctx:
        def sb(name, shape, dt=F32):
            return ctx.enter_context(nc.sbuf_tensor(name, shape, dt))

        def bank(name):
            return ctx.enter_context(nc.psum_tensor(name, [P, 512], F32))

        def sem(name):
            return ctx.enter_context(nc.semaphore(name))

        tables = sb("tables", [P, 3 * P + C + 1])
        ident = tables[:, 0:P]
        side_mask = tables[0:EDGE, P:3 * P].rearrange("p (s n) -> p s n", s=2)
        chunk_mask = tables[:, 3 * P:3 * P + C]
        lo_rows = tables[:, 3 * P + C:3 * P + C + 1]
        w = sb("w", [P, N_REL, OUT])
        w_hi = sb("w_hi", [P, N_REL, OUT], F32R)
        w_lo = sb("w_lo", [P, N_REL, OUT], F32R)
        w_edge = sb("w_edge", [EDGE, N_REL, OUT])
        edges = sb("edges", [EDGE, N_REL])
        edge_lhs = sb("edge_lhs", [EDGE, len(OUTER), P])
        c_hi = sb("c_hi", [P, len(OUTER), OUT], F32R)
        c_rows = sb("c_rows", [P, len(OUTER), OUT], F32R)
        c_col = sb("c_col", [P, len(X_RELS)])
        bias = sb("bias", [P, C, OUT])
        neg_half = sb("neg_half", [P, C])
        zeros = sb("zeros", [P, 2 * C])

        blocks = [sb(f"blocks{n}", [P, NODES // Q, P]) for n in range(2)]
        at = [sb(f"at{n}", [P, C, NODES]) for n in range(2)]
        a = [sb(f"a{n}", [P, C, NODES]) for n in range(2)]
        a_hi = [sb(f"a_hi{n}", [P, C, NODES], F32R) for n in range(2)]
        a_lo = [sb(f"a_lo{n}", [P, C, NODES], F32R) for n in range(2)]
        at_hi = [sb(f"at_hi{n}", [P, C, NODES], F32R) for n in range(2)]
        at_lo = [sb(f"at_lo{n}", [P, C, NODES], F32R) for n in range(2)]
        xs = [sb(f"xs{n}", [P, C, FEAT]) for n in range(2)]
        x_hi = [sb(f"x_hi{n}", [P, C, FEAT], F32R) for n in range(2)]
        x_lo = [sb(f"x_lo{n}", [P, C, FEAT], F32R) for n in range(2)]
        xt_hi = [sb(f"xt_hi{n}", [P, NODES], F32R) for n in range(2)]
        xt_lo = [sb(f"xt_lo{n}", [P, NODES], F32R) for n in range(2)]
        xb = [sb(f"xb{n}", [P, C, FEAT]) for n in range(2)]
        sums = [sb(f"sums{n}", [P, 2 * C]) for n in range(2)]
        sum_parts = [sb(f"sum_parts{n}", [P, P]) for n in range(2)]
        o = [sb(f"o{n}", [P, C, OUT]) for n in range(2)]
        sums_hi = sb("sums_hi", [P, 2 * C], F32R)
        sum_rows = sb("sum_rows", [P, NODES], F32R)
        zt_hi = sb("zt_hi", [P, NODES], F32R)
        zt_lo = sb("zt_lo", [P, NODES], F32R)
        yt_hi = sb("yt_hi", [P, NODES], F32R)
        yt_lo = sb("yt_lo", [P, NODES], F32R)
        best = sb("best", [P, NODES])
        best_by_chunk = sb("best_by_chunk", [P, NODES])
        t = sb("t", [P, C, OUT])
        stats = sb("stats", [P, C, 6])
        mean_var = sb("mean_var", [P, C, 2])
        var_eps = sb("var_eps", [P, C])
        rstd = sb("rstd", [P, C])
        shift = sb("shift", [P, C])

        z_ps, y_ps = bank("z_ps"), bank("y_ps")
        rel_ps = [bank(f"rel_ps{n}") for n in range(4)]
        xt_ps = bank("xt_ps")
        misc_ps = bank("misc_ps")

        tables_in = sem("tables_in")
        w_in = sem("w_in")
        bias_in = sem("bias_in")
        edges_in = sem("edges_in")
        x_in = [sem("x_in0"), sem("x_in1")]
        a_in = [sem("a_in0"), sem("a_in1")]
        blocks_in = [sem("blocks_in0"), sem("blocks_in1")]
        stored = [sem("stored0"), sem("stored1")]
        w_hi_done = sem("w_hi_done")
        w_lo_done = sem("w_lo_done")
        pads_zero = sem("pads_zero")
        edge_lhs_done = sem("edge_lhs_done")
        c_mm = sem("c_mm")
        c_hi_done = sem("c_hi_done")
        c_done = sem("c_done")
        a_hi_done = sem("a_hi_done")
        a_lo_done = sem("a_lo_done")
        at_tr = sem("at_tr")
        at_hi_done = sem("at_hi_done")
        at_lo_v = sem("at_lo_v")
        at_lo_g = sem("at_lo_g")
        x_hi_done = sem("x_hi_done")
        x_lo_done = sem("x_lo_done")
        xb_done = sem("xb_done")
        xt_tr = sem("xt_tr")
        xt_hi_done = sem("xt_hi_done")
        xt_lo_done = sem("xt_lo_done")
        sums_hi_done = sem("sums_hi_done")
        parts_done = sem("parts_done")
        sums_tr = sem("sums_tr")
        sum_rows_done = sem("sum_rows_done")
        z_mm = sem("z_mm")
        zt_hi_done = sem("zt_hi_done")
        zt_lo_done = sem("zt_lo_done")
        y_mm = sem("y_mm")
        yt_hi_done = sem("yt_hi_done")
        yt_lo_done = sem("yt_lo_done")
        rel_mm = sem("rel_mm")
        first_done = sem("first_done")
        max_done = sem("max_done")
        back_tr = sem("back_tr")
        t_done = sem("t_done")
        stats_done = sem("stats_done")
        mean_done = sem("mean_done")
        var_done = sem("var_done")
        rstd_done = sem("rstd_done")
        shift_done = sem("shift_done")
        o_done = sem("o_done")
        o_last_done = sem("o_last_done")

        block = ctx.enter_context(nc.Block())

        def after(eng, s, value):
            if not isinstance(value, int) or value > 0:
                eng.wait_ge(s, value)

        def graphs(eng, step):
            step(0, 0, True, False)
            with eng.Fori(0, GRAPHS // 2 - 1) as h:
                step(h, 1, True, True)
                step(h + 1, 0, True, True)
            step(GRAPHS // 2 - 1, 1, False, True)

        def following(half, odd):
            return (half + 1, 0) if odd else (half, 1)

        @block.sync
        def _(sp):
            def four(dst, src, s):
                for q in range(4):
                    sp.dma_start(dst[q * Q:(q + 1) * Q], src[q]).then_inc(s, 16)

            def load(odd, graph, after_first=False):
                after(sp, a_hi_done, C * (graph - 1))
                after(sp, a_lo_done, C * (graph - 2))
                if after_first:
                    sp.wait_ge(z_mm, 1)
                four(a[odd], adj_d[graph], a_in[odd])
                after(sp, at_tr, C * (graph - 1))
                four(blocks[odd], blocks_d[graph], blocks_in[odd])
                after(sp, x_lo_done, graph - 2)
                after(sp, xt_tr, graph - 1)
                after(sp, xb_done, graph - 1)
                after(sp, y_mm, graph - 1)
                four(xs[odd], x_d[graph], x_in[odd])

            def store(odd, graph):
                after(sp, o_done, C * (graph + 1))
                for q in range(4):
                    sp.dma_start(out_d[graph][q], o[odd][q * Q:(q + 1) * Q]).then_inc(stored[odd], 16)

            four(xs[0], x_d[0], x_in[0])
            four(a[0], adj_d[0], a_in[0])
            four(blocks[0], blocks_d[0], blocks_in[0])
            sp.dma_start(w[:], W[:, 0:FEAT, :].rearrange("r f o -> f r o")).then_inc(w_in, 16)
            load(1, 1)
            four(bias, bias_d, bias_in)
            load(0, 2, after_first=True)
            with sp.Fori(0, GRAPHS // 2 - 2) as h:
                load(1, 2 * h + 3)
                store(0, 2 * h)
                load(0, 2 * h + 4)
                store(1, 2 * h + 1)
            last = GRAPHS // 2 - 1
            load(1, 2 * last + 1)
            for graph in range(2 * last - 2, GRAPHS - 1):
                store(graph % 2, graph)
            for done, before, chunks in ((o_last_done, 0, LAST_ON_VECTOR), (o_done, C * (GRAPHS - 1), LAST_ON_SCALAR)):
                for n, j in enumerate(chunks):
                    sp.wait_ge(done, before + n + 1)
                    sp.dma_start(out_d[GRAPHS - 1][:, :, j], o[1][:, j, :]).then_inc(stored[1], 16)
            for s in stored:
                sp.wait_ge(s, 64 * (GRAPHS // 2))

        @block.scalar
        def _(act):
            def split_a(half, odd, j):
                g = 2 * half + odd
                if j == 0:
                    act.wait_ge(a_in[odd], 64 * (half + 1))
                    after(act, z_mm, g - 1)
                    after(act, parts_done, 2 * (g - 1))
                act.activation(a_hi[odd][:, j, :], a[odd][:, j, :], ACT.Copy,
                               accum_out=sums[odd][:, j:j + 1]).then_inc(a_hi_done, 1)

            def split_at(half, odd, k):
                g = 2 * half + odd
                act.wait_ge(at_tr, C * g + k + 1)
                if k == 0:
                    after(act, y_mm, g - 1)
                    after(act, parts_done, 2 * (g - 1))
                act.activation(at_hi[odd][:, k, :], at[odd][:, k, :], ACT.Copy,
                               accum_out=sums[odd][:, C + k:C + k + 1]).then_inc(at_hi_done, 1)

            def split_xt(half, odd):
                act.wait_ge(xt_tr, 2 * half + odd + 1)
                act.activation(xt_hi[odd][:], xt_ps[:], ACT.Copy).then_inc(xt_hi_done, 1)

            def round_x(half, odd):
                act.wait_ge(x_in[odd], 64 * (half + 1))
                after(act, y_mm, 2 * half + odd - 1)
                act.activation(x_hi[odd][:], xs[odd][:], ACT.Copy).then_inc(x_hi_done, 1)

            def normalize(half, odd, chunks=range(C)):
                g = 2 * half + odd
                act.wait_ge(shift_done, g + 1)
                after(act, stored[odd], 64 * half)
                for j in chunks:
                    act.activation(o[odd][:, j, :], t[:, j, :], ACT.Identity, bias=shift[:, j:j + 1],
                                   scale=rstd[:, j:j + 1]).then_inc(o_done, 1)

            split_xt(0, 0)
            for j in range(C):
                split_a(0, 0, j)
            act.wait_ge(w_in, 16)
            act.activation(w_hi[:], w[:], ACT.Copy).then_inc(w_hi_done, 1)
            for k in range(C):
                split_at(0, 0, k)

            def split_z(g):
                act.wait_ge(z_mm, g + 1)
                act.activation(zt_hi[:], z_ps[:], ACT.Copy).then_inc(zt_hi_done, 1)

            def split_y(g):
                act.wait_ge(y_mm, g + 1)
                act.activation(yt_hi[:], y_ps[:], ACT.Copy).then_inc(yt_hi_done, 1)

            def spread_sums(g):
                act.wait_ge(sums_tr, g + 1)
                after(act, rel_mm, NR * g)
                for k in range(C):
                    act.activation(sum_rows[:].rearrange("p (q k c) -> p k q c", q=4, k=C)[:, k],
                                   misc_ps[:, 0:P].rearrange("p (q c) -> p q c", q=4), ACT.Copy,
                                   scale=chunk_mask[:, k:k + 1]).then_inc(sum_rows_done, 1)

            def start_max(g):
                act.wait_ge(rel_mm, NR * g + 1)
                act.activation(best[:], rel_ps[0][:], ACT.Identity, bias=c_col[:, 0:1]).then_inc(first_done, 1)

            def step(half, odd, early, late):
                g = 2 * half + odd
                nxt = following(half, odd)
                prev = (half, 0) if odd else (half - 1, 1)
                if not late:
                    split_z(g)
                    split_a(*nxt, 0)
                    split_a(*nxt, 1)
                    split_a(*nxt, 2)
                    split_a(*nxt, 3)
                    round_x(*nxt)
                    split_y(g)
                    act.wait_ge(c_done, 2)
                    start_max(g)
                    spread_sums(g)
                    split_at(*nxt, 0)
                    split_at(*nxt, 1)
                    split_xt(*nxt)
                    split_at(*nxt, 2)
                    split_at(*nxt, 3)
                    return
                if early:
                    split_a(*nxt, 0)
                    round_x(*nxt)
                    split_a(*nxt, 1)
                    split_a(*nxt, 2)
                    split_at(*nxt, 0)
                split_z(g)
                if early:
                    split_a(*nxt, 3)
                    split_at(*nxt, 1)
                spread_sums(g)
                split_y(g)
                start_max(g)
                if early:
                    split_at(*nxt, 2)
                if early:
                    split_xt(*nxt)
                    split_at(*nxt, 3)
                normalize(*prev)

            graphs(act, step)
            normalize(GRAPHS // 2 - 1, 1, LAST_ON_SCALAR)

        @block.vector
        def _(dve):
            def transpose_a(half, odd, k):
                g = 2 * half + odd
                if k == 0:
                    dve.wait_ge(blocks_in[odd], 64 * (half + 1))
                    after(dve, at_hi_done, C * (g - 1))
                    after(dve, at_lo_g, len(ON_GPSIMD) * (g - 2))
                    after(dve, at_lo_v, len(ON_VECTOR) * (g - 2))
                    after(dve, y_mm, g - 1)
                dve.transpose(at[odd][:, k, :], blocks[odd][:, :, k * Q:(k + 1) * Q]).then_inc(at_tr, 1)

            def split_at(half, odd, k):
                g = 2 * half + odd
                dve.wait_ge(at_hi_done, C * g + k + 1)
                after(dve, y_mm, g - 1)
                dve.tensor_tensor(at_lo[odd][:, k, :], at[odd][:, k, :], at_hi[odd][:, k, :].bitcast(F32),
                                  ALU.subtract).then_inc(at_lo_v, 1)

            def split_xt(half, odd):
                dve.wait_ge(xt_hi_done, 2 * half + odd + 1)
                dve.tensor_tensor(xt_lo[odd][:], xt_ps[:], xt_hi[odd][:].bitcast(F32),
                                  ALU.subtract).then_inc(xt_lo_done, 1)

            for n in range(2):
                dve.memset(sum_parts[n][:], 0.0).then_inc(pads_zero, 1)
            dve.memset(neg_half[:], -0.5).then_inc(pads_zero, 1)
            dve.memset(zeros[:], 0.0).then_inc(pads_zero, 1)
            dve.wait_ge(tables_in, 16)
            dve.wait_ge(edges_in, 2 * 16)
            for n, r in enumerate(OUTER):
                dve.tensor_scalar(edge_lhs[:, n, :], side_mask[:, 0 if r in Y_RELS else 1, :], edges[:, r:r + 1],
                                  None, ALU.mult).then_inc(edge_lhs_done, 1)
            split_xt(0, 0)
            for k in range(C):
                transpose_a(0, 0, k)
            dve.wait_ge(c_mm, 1)
            dve.tensor_copy(c_hi[:], misc_ps[:]).then_inc(c_hi_done, 1)
            dve.tensor_copy(c_col[:], xt_ps[:, 0:len(X_RELS)]).then_inc(c_done, 1)
            dve.wait_ge(c_hi_done, 1)
            dve.scalar_tensor_tensor(out=c_rows[:], in0=c_hi[:].bitcast(F32), scalar=lo_rows,
                                     in1=misc_ps[:].rearrange("p (r o) -> p r o", o=OUT),
                                     op0=ALU.mult, op1=ALU.add).then_inc(c_done, 1)
            dve.wait_ge(w_hi_done, 1)
            dve.tensor_tensor(w_lo[:], w[:], w_hi[:].bitcast(F32), ALU.subtract).then_inc(w_lo_done, 1)

            def take_max(g, q):
                dve.wait_ge(rel_mm, NR * g + q + 1)
                if q == 1:
                    dve.wait_ge(first_done, g + 1)
                else:
                    dve.wait_ge(max_done, (NR - 1) * g + q - 1)
                ps = rel_ps[q % 4][:]
                if q < len(X_RELS):
                    op = dve.scalar_tensor_tensor(out=best[:], in0=ps, scalar=c_col[:, q:q + 1], in1=best[:],
                                                  op0=ALU.add, op1=ALU.max)
                elif q < NR - 1:
                    op = dve.tensor_tensor(best[:], ps, best[:], ALU.max)
                else:
                    after(dve, back_tr, g)
                    nodes = "p (q k c) -> p q k c"
                    op = dve.tensor_tensor(best_by_chunk[:].rearrange("p (k q c) -> p q k c", k=C, q=4),
                                           ps.rearrange(nodes, q=4, k=C), best[:].rearrange(nodes, q=4, k=C),
                                           ALU.max)
                op.then_inc(max_done, 1)

            def add_residual(half, odd):
                g = 2 * half + odd
                dve.wait_ge(back_tr, g + 1)
                dve.wait_ge(xb_done, g + 1)
                after(dve, o_done, C * g)
                dve.tensor_tensor(t[:], misc_ps[:].rearrange("p (j f) -> p j f", j=C), xb[odd][:],
                                  ALU.add).then_inc(t_done, 1)

            def statistics(half, odd):
                g = 2 * half + odd
                dve.wait_ge(t_done, g + 1)
                after(dve, mean_done, C * g)
                for j in range(C):
                    dve.bn_stats(stats[:, j, :], t[:, j, :]).then_inc(stats_done, 1)

            def wait_stats(half, odd):
                g = 2 * half + odd
                dve.wait_ge(stats_done, C * (g + 1))

            def mean_and_variance():
                for j in range(C):
                    dve.bn_aggr(mean_var[:, j, :], stats[:, j, :]).then_inc(mean_done, 1)

            def add_eps(half, odd):
                g = 2 * half + odd
                dve.wait_ge(mean_done, C * (g + 1))
                after(dve, rstd_done, g)
                dve.tensor_scalar(var_eps[:], mean_var[:, :, 1], EPS, None, ALU.add).then_inc(var_done, 1)

            def negative_shift(half, odd):
                g = 2 * half + odd
                dve.wait_ge(rstd_done, g + 1)
                dve.scalar_tensor_tensor(out=shift[:], in0=mean_var[:, :, 0], scalar=-1.0, in1=rstd[:],
                                         op0=ALU.mult, op1=ALU.mult).then_inc(shift_done, 1)

            def split_z(g):
                dve.wait_ge(zt_hi_done, g + 1)
                dve.tensor_tensor(zt_lo[:], z_ps[:], zt_hi[:].bitcast(F32), ALU.subtract).then_inc(zt_lo_done, 1)

            def split_y(g):
                dve.wait_ge(yt_hi_done, g + 1)
                dve.tensor_tensor(yt_lo[:], y_ps[:], yt_hi[:].bitcast(F32), ALU.subtract).then_inc(yt_lo_done, 1)

            def step(half, odd, early, late):
                g = 2 * half + odd
                nxt = following(half, odd)
                prev = (half, 0) if odd else (half - 1, 1)
                if not late:
                    split_z(g)
                    transpose_a(*nxt, 0)
                    transpose_a(*nxt, 1)
                    split_y(g)
                    take_max(g, 1)
                    take_max(g, 2)
                    take_max(g, 3)
                    transpose_a(*nxt, 2)
                    take_max(g, 4)
                    transpose_a(*nxt, 3)
                    take_max(g, 5)
                    take_max(g, 6)
                    for k in ON_VECTOR:
                        split_at(*nxt, k)
                    split_xt(*nxt)
                    return
                if early:
                    transpose_a(*nxt, 0)
                add_residual(*prev)
                if early:
                    transpose_a(*nxt, 1)
                statistics(*prev)
                if early:
                    transpose_a(*nxt, 2)
                wait_stats(*prev)
                split_z(g)
                mean_and_variance()
                add_eps(*prev)
                if early:
                    transpose_a(*nxt, 3)
                split_y(g)
                take_max(g, 1)
                negative_shift(*prev)
                take_max(g, 2)
                if early:
                    split_xt(*nxt)
                take_max(g, 3)
                take_max(g, 4)
                take_max(g, 5)
                take_max(g, 6)
                if early:
                    for k in ON_VECTOR:
                        split_at(*nxt, k)

            graphs(dve, step)
            add_residual(GRAPHS // 2 - 1, 1)
            statistics(GRAPHS // 2 - 1, 1)
            wait_stats(GRAPHS // 2 - 1, 1)
            mean_and_variance()
            add_eps(GRAPHS // 2 - 1, 1)
            negative_shift(GRAPHS // 2 - 1, 1)
            dve.wait_ge(stored[1], 64 * (GRAPHS // 2 - 1))
            dve.wait_ge(shift_done, GRAPHS)
            for j in LAST_ON_VECTOR:
                dve.tensor_scalar(o[1][:, j, :], t[:, j, :], rstd[:, j:j + 1], shift[:, j:j + 1],
                                  ALU.mult, ALU.add).then_inc(o_last_done, 1)

        @block.gpsimd
        def _(pool):
            def split_a(half, odd, j):
                g = 2 * half + odd
                pool.wait_ge(a_hi_done, C * g + j + 1)
                if j == 0:
                    after(pool, z_mm, g - 1)
                pool.tensor_tensor(a_lo[odd][:, j, :], a[odd][:, j, :], a_hi[odd][:, j, :].bitcast(F32),
                                   ALU.subtract).then_inc(a_lo_done, 1)

            def split_at(half, odd, k):
                g = 2 * half + odd
                pool.wait_ge(at_hi_done, C * g + k + 1)
                after(pool, y_mm, g - 1)
                pool.tensor_tensor(at_lo[odd][:, k, :], at[odd][:, k, :], at_hi[odd][:, k, :].bitcast(F32),
                                   ALU.subtract).then_inc(at_lo_g, 1)

            def split_x(half, odd):
                g = 2 * half + odd
                pool.wait_ge(x_hi_done, g)
                after(pool, y_mm, g - 1)
                pool.tensor_tensor(x_lo[odd][:], xs[odd][:], x_hi[odd][:].bitcast(F32),
                                   ALU.subtract).then_inc(x_lo_done, 1)

            def split_sums(half, odd):
                g = 2 * half + odd
                n = 2 * C
                pool.wait_ge(a_hi_done, C * (g + 1))
                pool.wait_ge(at_hi_done, C * (g + 1))
                after(pool, parts_done, 2 * g)
                after(pool, sums_tr, g - 1)
                pool.tensor_tensor(sums_hi[:], sums[odd][:], zeros[:], ALU.add).then_inc(sums_hi_done, 1)
                pool.wait_ge(sums_hi_done, g + 1)
                parts = sum_parts[odd][:, 0:4 * n].rearrange("p (b a n) -> p b a n", b=2, n=n)
                pool.tensor_tensor(parts[:, 0, 1, :], sums[odd][:], sums_hi[:].bitcast(F32),
                                   ALU.subtract).then_inc(parts_done, 1)
                pool.tensor_copy(parts[:, :, 0, :],
                                 sums_hi[:].bitcast(F32).rearrange("p (a n) -> p a n", a=1).to_broadcast([P, 2, n])
                                 ).then_inc(parts_done, 1)

            def add_bias(half, odd):
                g = 2 * half + odd
                pool.wait_ge(x_in[odd], 64 * (half + 1))
                after(pool, t_done, g - 1)
                pool.tensor_tensor(xb[odd][:], xs[odd][:], bias[:], ALU.add).then_inc(xb_done, 1)

            def inverse_deviation(half, odd):
                g = 2 * half + odd
                pool.wait_ge(var_done, g + 1)
                after(pool, o_done, C * g)
                pool.tensor_tensor(rstd[:], var_eps[:], neg_half[:], ALU.pow).then_inc(rstd_done, 1)

            pool.dma_start(tables[:], tables_d).then_inc(tables_in, 16)
            with nc.allow_non_contiguous_dma(reason="112 numbers"):
                pool.dma_start(edges[:], W_edges.rearrange("r d -> d r")).then_inc(edges_in, 16)
            pool.dma_start(w_edge[:], W[:, FEAT:K_ALL, :].rearrange("r d o -> d r o")).then_inc(edges_in, 16)
            pool.wait_ge(pads_zero, 4)
            split_sums(0, 0)

            def step(half, odd, early, late):
                nxt = following(half, odd)
                prev = (half, 0) if odd else (half - 1, 1)
                if early:
                    if not late:
                        split_a(*nxt, 0)
                        split_a(*nxt, 1)
                    split_x(*nxt)
                    for j in range(0 if late else 2, C - 1):
                        split_a(*nxt, j)
                if late:
                    inverse_deviation(*prev)
                if early:
                    split_a(*nxt, C - 1)
                    if not late:
                        pool.wait_ge(bias_in, 4 * 16)
                        add_bias(half, odd)
                    for k in ON_GPSIMD:
                        split_at(*nxt, k)
                    split_sums(*nxt)
                    add_bias(*nxt)

            graphs(pool, step)
            inverse_deviation(GRAPHS // 2 - 1, 1)

        @block.tensor
        def _(pe):
            def transpose_x(half, odd):
                g = 2 * half + odd
                pe.wait_ge(x_in[odd], 64 * (half + 1))
                after(pe, xt_lo_done, g)
                for k in range(C):
                    op = pe.transpose(xt_ps[:].rearrange("p (q k c) -> p k q c", q=4, k=C)[:, k], xs[odd][:, k, :],
                                      ident)
                op.then_inc(xt_tr, 1)

            def transpose_back(g):
                pe.wait_ge(max_done, (NR - 1) * (g + 1))
                for j in range(C):
                    op = pe.transpose(misc_ps[:, j * P:(j + 1) * P],
                                      best_by_chunk[:, j * P:(j + 1) * P], ident)
                op.then_inc(back_tr, 1)

            def transpose_sums(half, odd):
                g = 2 * half + odd
                pe.wait_ge(parts_done, 2 * (g + 1))
                after(pe, t_done, g)
                pe.transpose(misc_ps[:, 0:P], sum_parts[odd][:], ident).then_inc(sums_tr, 1)

            def product(ps, w_parts, v_parts, start, stop):
                (wh, wl), (vh, vl) = w_parts, v_parts
                pe.matmul(ps, wh, vh, start=start, stop=False)
                pe.matmul(ps, wh, vl, start=False, stop=False)
                return pe.matmul(ps, wl, vh, start=False, stop=stop)

            def constants():
                pe.wait_ge(edge_lhs_done, len(OUTER))
                for n, r in enumerate(OUTER):
                    pe.matmul(misc_ps[:, n * OUT:(n + 1) * OUT], edge_lhs[:, n, :], w_edge[:, r, :],
                              start=True, stop=True)
                pe.wait_ge(xt_lo_done, 1)
                for n, r in enumerate(X_RELS):
                    op = pe.matmul(xt_ps[:, n:n + 1], w_edge[:, r, :], edges[:, r:r + 1], start=True, stop=True)
                op.then_inc(c_mm, 1)

            pe.wait_ge(tables_in, 16)
            transpose_x(0, 0)

            def step(half, odd, early, late):
                g = 2 * half + odd
                nxt = following(half, odd)
                if late:
                    pe.wait_ge(x_lo_done, g)
                else:
                    pe.wait_ge(a_in[odd], 64)
                after(pe, zt_lo_done, g)
                for j in range(C):
                    first, last = j == 0, j == C - 1
                    if late:
                        pe.wait_ge(a_lo_done, C * (g - 1) + j + 1)
                        op = product(z_ps[:], (x_hi[odd][:, j, :], x_lo[odd][:, j, :]),
                                     (a_hi[odd][:, j, :], a_lo[odd][:, j, :]), first, last)
                    else:
                        op = pe.matmul(z_ps[:], xs[odd][:, j, :], a[odd][:, j, :], start=first, stop=last)
                    if j == C - 1:
                        op.then_inc(z_mm, 1)
                if late:
                    pe.wait_ge(sum_rows_done, C * g)
                    transpose_back(g - 1)
                else:
                    constants()
                after(pe, yt_lo_done, g)
                for k in range(C):
                    first, last = k == 0, k == C - 1
                    if not late:
                        pe.wait_ge(at_tr, C * g + k + 1)
                        op = pe.matmul(y_ps[:], xs[odd][:, k, :], at[odd][:, k, :], start=first, stop=last)
                    else:
                        if k in ON_VECTOR:
                            pe.wait_ge(at_lo_v, len(ON_VECTOR) * (g - 1) + ON_VECTOR.index(k) + 1)
                        else:
                            pe.wait_ge(at_lo_g, len(ON_GPSIMD) * (g - 1) + ON_GPSIMD.index(k) + 1)
                        op = product(y_ps[:], (x_hi[odd][:, k, :], x_lo[odd][:, k, :]),
                                     (at_hi[odd][:, k, :], at_lo[odd][:, k, :]), first, last)
                    if k == C - 1:
                        op.then_inc(y_mm, 1)
                    if k == 2 and late:
                        transpose_sums(half, odd)
                if not late:
                    pe.wait_ge(w_lo_done, 1)
                for q, r in enumerate(RELS):
                    if q == 0:
                        after(pe, max_done, (NR - 1) * g)
                    elif q == 4:
                        pe.wait_ge(first_done, g + 1)
                    elif q > 4:
                        pe.wait_ge(max_done, (NR - 1) * g + q - 4)
                    if q == 0:
                        pe.wait_ge(xt_lo_done, g + 1)
                    if r in X_RELS:
                        v_parts = (xt_hi[odd][:], xt_lo[odd][:])
                    elif r in Z_RELS:
                        pe.wait_ge(zt_lo_done, g + 1)
                        pe.wait_ge(sum_rows_done, C * (g + 1))
                        v_parts = (zt_hi[:], zt_lo[:])
                    else:
                        pe.wait_ge(yt_lo_done, g + 1)
                        v_parts = (yt_hi[:], yt_lo[:])
                    ps = rel_ps[q % 4][:]
                    op = product(ps, (w_hi[:, r, :], w_lo[:, r, :]), v_parts, True, r in X_RELS)
                    if r in OUTER:
                        op = pe.matmul(ps, c_rows[:, OUTER.index(r), :], sum_rows[:], start=False, stop=True)
                    op.then_inc(rel_mm, 1)
                    if q == 0 and not late:
                        pe.wait_ge(c_done, 2)
                        transpose_sums(half, odd)
                    if early and q == 1:
                        transpose_x(*nxt)

            graphs(pe, step)
            transpose_back(GRAPHS - 1)


def kernel(x, adj, L0_gnn_W, L0_gnn_W_edges, L0_gnn_b):
    import numpy as np
    import concourse.bacc as bacc
    from concourse.bass_utils import run_bass_kernel_spmd

    row = np.arange(P)
    used = row < ROWS
    sides = np.broadcast_to((used & (row // 4 % 2 == np.arange(2)[:, None])).reshape(1, 2 * P), (P, 2 * P))
    chunks = used[:, None] & (row[:, None] % 4 == np.arange(4))
    lo_rows = -1.0 * (used & (row // 8 == 2))[:, None]
    arrays = {
        "x": x, "adj": adj, "w": L0_gnn_W, "w_edges": L0_gnn_W_edges, "b": L0_gnn_b,
        "tables": np.concatenate([np.eye(P), sides, chunks, lo_rows], axis=1, dtype=np.float32),
    }
    arrays = {f"in_{k}_dram": np.ascontiguousarray(v) for k, v in arrays.items()}
    nc = bacc.Bacc("TRN2", target_bir_lowering=False, num_devices=1)
    args = [nc.dram_tensor(k, v.shape, mybir.dt.from_np(v.dtype), kind="ExternalInput").ap()
            for k, v in arrays.items()]
    out = nc.dram_tensor("out_dram", x.shape, F32, kind="ExternalOutput").ap()
    graph_layer(nc, *args, out)
    r = run_bass_kernel_spmd(nc, [arrays], core_ids=[0])
    return r.results[0]["out_dram"]
```
